# Optimizing a Trainium2 kernel written in Bass

```python
import numpy as np
import jax
import jax.numpy as jnp

def _softmax(x, axis=-1):
    return jax.nn.softmax(x, axis=axis)

def _gelu(x):
    return jax.nn.gelu(x, approximate=True)

def _silu(x):
    return jax.nn.silu(x)

def _sigmoid(x):
    return jax.nn.sigmoid(x)

def _layernorm(x, axis=-1, eps=1e-05):
    m = jnp.mean(x, axis=axis, keepdims=True)
    v = jnp.var(x, axis=axis, keepdims=True)
    return (x - m) / jnp.sqrt(v + eps)

def _scatter_add(tgt, idx, src, axis=0):
    return tgt.at[idx].add(src)

def _segment_sum(src, seg, n):
    return jax.ops.segment_sum(src, seg, n)
kernel_name = 'mk_conv_preact_d1_conv_nchw2048_r4_e35d4c'

def setup_inputs(seed: int=0):
    np.random.seed(seed)
    _w = jnp.asarray

    def _rec_inputs():
        import jax
        import jax.numpy as jnp
        _gk = jax.random.key(seed)
        x = -0.0004039 + 1 * jax.random.normal(jax.random.fold_in(_gk, 1), (4, 512, 32, 48), jnp.float32)
        return x
    x = _rec_inputs()

    def _L0_conv_setup():
        import jax, jax.numpy as jnp
        import numpy as np
        key = jax.random.key(seed)
        k1, k2, k3 = jax.random.split(key, 3)
        N, C, H, W = (4, 512, 32, 48)
        feature = jax.random.normal(k1, (N, C, H, W), dtype=jnp.float32)
        conv_w = jax.random.normal(k2, (C, C, 1, 9), dtype=jnp.float32) * 0.01
        conv_b = jax.random.normal(k3, (C,), dtype=jnp.float32) * 0.01
        prelu_a = jnp.asarray(0.25, dtype=jnp.float32)
        return {'feature': feature, 'conv_w': conv_w, 'conv_b': conv_b, 'prelu_a': prelu_a}
    _L0_conv_all = _L0_conv_setup()
    _L0_conv_in = {k: v for k, v in _L0_conv_all.items() if k in ('conv_w', 'conv_b', 'prelu_a')}
    del _L0_conv_all
    return {'x': x, 'L0_conv_conv_w': _L0_conv_in['conv_w'], 'L0_conv_conv_b': _L0_conv_in['conv_b'], 'L0_conv_prelu_a': _L0_conv_in['prelu_a']}

def reference(x, L0_conv_conv_w, L0_conv_conv_b, L0_conv_prelu_a):
    import jax
    import jax.numpy as jnp

    def _L0_conv_ref(feature, conv_w, conv_b, prelu_a):
        import jax, jax.numpy as jnp
        import numpy as np
        Wc = conv_w[:, :, 0, 4]

        def step(prev, x_i):
            y = jnp.einsum('oc,nch->noh', Wc, prev) + conv_b[None, :, None]
            y = jnp.where(y >= 0, y, prelu_a * y)
            cur = y + x_i
            return (cur, cur)
        x = jnp.moveaxis(feature, 3, 0)
        _, fwd_rest = jax.lax.scan(step, x[0], x[1:])
        fl = jnp.concatenate([x[0:1], fwd_rest], axis=0)
        _, bwd_rest = jax.lax.scan(step, fl[-1], fl[:-1], reverse=True)
        out = jnp.concatenate([bwd_rest, fl[-1:]], axis=0)
        return jnp.moveaxis(out, 0, 3)

    def _gn(v, G=32, eps=1e-05):
        B_, C_, H_, W_ = v.shape
        g = v.reshape(B_, G, C_ // G, H_, W_)
        m = jnp.mean(g, axis=(2, 3, 4), keepdims=True)
        s = jnp.var(g, axis=(2, 3, 4), keepdims=True)
        return ((g - m) / jnp.sqrt(s + eps)).reshape(v.shape)

    def _ln_c(v, eps=1e-06):
        m = jnp.mean(v, axis=1, keepdims=True)
        s = jnp.var(v, axis=1, keepdims=True)
        return (v - m) / jnp.sqrt(s + eps)

    def _ln_t(v, eps=1e-05):
        m = jnp.mean(v, axis=-1, keepdims=True)
        s = jnp.var(v, axis=-1, keepdims=True)
        return (v - m) / jnp.sqrt(s + eps)

    def _to_tokens(v):
        B_, C_, H_, W_ = v.shape
        return v.reshape(B_, C_, H_ * W_).transpose(0, 2, 1)

    def _from_tokens(t, like):
        B_, C_, H_, W_ = like.shape
        return t.transpose(0, 2, 1).reshape(B_, C_, H_, W_)
    x = x + _L0_conv_ref(_gn(x), L0_conv_conv_w, L0_conv_conv_b, L0_conv_prelu_a)
    return x

_drawn_inputs = setup_inputs


def setup_inputs(seed=0):
    import zlib

    import numpy as np

    out = dict(_drawn_inputs(seed))
    spreads = {}
    factors = {'L0_conv_conv_b': 8.0}
    for name, (base, spread) in spreads.items():
        noise = np.random.default_rng([zlib.crc32(name.encode()), seed]).standard_normal(out[name].shape)
        drawn = base * np.exp(spread * noise) if base else spread * noise
        out[name] = jnp.asarray(drawn.astype(out[name].dtype))
    for name, factor in factors.items():
        out[name] = (out[name] * factor).astype(out[name].dtype)
    return out
```

```python
from contextlib import ExitStack

import concourse.bass as bass
from concourse import mybir

ALU = mybir.AluOpType
ACT = mybir.ActivationFunctionType
AXIS = mybir.AxisListType
F32 = mybir.dt.float32
F32R = mybir.dt.float32r

P = 128
GROUP = 16
EPS = 1e-5
SKEW = 8

UNITS = [(0, 0), (0, 1), (0, 2), (0, 3), (1, 0), (1, 1), (2, 0), (3, 0),
         (2, 1), (3, 1), (1, 2), (2, 2), (3, 2), (1, 3), (2, 3), (3, 3)]


def scan_program(nc, x, conv_w, conv_b, prelu_a, out):
    N, C, H, W = x.shape
    KT = C // P
    NG = N // 2
    COLS = NG * H
    TAPS = conv_w.shape[3]
    MID = TAPS // 2
    STEPS = 2 * (W - 1)
    FWD = W - 1
    LAST = STEPS + SKEW
    FEAT = KT * COLS
    BLK = H * W
    CHUNK = 12
    NBLK = KT * NG
    STAT = 512
    NSTAT = BLK // STAT
    assert KT == 4 and N == 4 and W % CHUNK == 0 and SKEW < CHUNK and SKEW % 2 == 0 and FWD % 2 == 1

    with ExitStack() as ctx:
        def sb(name, shape, dt=F32):
            return ctx.enter_context(nc.sbuf_tensor(name, shape, dt))

        def sem(name):
            return ctx.enter_context(nc.semaphore(name))

        xio = sb("xio", [P, 2, KT, COLS, W])
        state = sb("state", [P, 2, W, KT, COLS])
        w_t = sb("w_t", [P, KT, C])
        above = sb("above", [P, 2, KT, 2 * COLS])
        below = sb("below", [P, 2, KT, 2 * COLS])
        ident = sb("ident", [P, P])
        bias = sb("bias", [P, KT])
        neg_bias = sb("neg_bias", [P, KT])
        slope = sb("slope", [P, 1])
        neg_slope = sb("neg_slope", [P, 1])
        bstat = sb("bstat", [P, NBLK, NSTAT, 6])
        chan = sb("chan", [P, 2, 32])
        chan_t = sb("chan_t", [P, 2, 16])
        gsum = sb("gsum", [P, 2])
        gsum_t = sb("gsum_t", [P, 2, 16])
        gmean = sb("gmean", [P, 32])
        dev = sb("dev", [P, 32])
        gdev = sb("gdev", [P, 32])
        neg_mean = sb("neg_mean", [P, 2, NBLK])
        var_eps = sb("var_eps", [P, 2, NBLK])
        minus_half = sb("minus_half", [P, NBLK])
        rstd = sb("rstd", [P, 2, NBLK])
        psum = ctx.enter_context(nc.psum_tensor("psum", [P, 8, 512], F32))

        x_loaded = [sem(f"x_loaded{n}") for n in range(N)]
        w_loaded = [sem(f"w_loaded{o}") for o in range(KT)]
        small_loaded = sem("small_loaded")
        zeroed = sem("zeroed")
        ident_done = sem("ident_done")
        w_turned = sem("w_turned")
        w_ready = sem("w_ready")
        negated = sem("negated")
        stat_step = sem("stat_step")
        var_done = sem("var_done")
        rstd_done = sem("rstd_done")
        norm_a = sem("norm_a")
        norm_b = sem("norm_b")
        tile_done = sem("tile_done")
        above_done = sem("above_done")
        below_done = sem("below_done")
        part_done = sem("part_done")
        state_ready = sem("state_ready")
        out_ready = sem("out_ready")
        stored = sem("stored")

        SROW, XROW = 2 * W * FEAT, 2 * KT * COLS * W
        SHALF, XHALF = W * FEAT, KT * COLS * W

        def w_raw(o):
            t, room = (xio, XHALF) if o < 2 else (state, SHALF)
            base = room + (o % 2) * C * TAPS
            return bass.AP(t, base, [[SROW, P], [1, C * TAPS]])

        def w_raw_block(o, k):
            t, room = (xio, XHALF) if o < 2 else (state, SHALF)
            base = room + (o % 2) * C * TAPS + k * P * TAPS + MID
            return bass.AP(t, base, [[SROW, P], [TAPS, P]])

        def cols(mode):
            return {"A": slice(0, COLS), "B": slice(COLS, 2 * COLS), "AB": slice(0, 2 * COLS)}[mode]

        def halves(mode, wa, wb, base, step, whole, gap):
            if mode == "A":
                return wa * step + base, []
            if mode == "B":
                return wb * step + whole + base, []
            return wa * step + base, [[whole + gap * step, 2]]

        def state_tile(mode, wa, wb, gap, o):
            off, half = halves(mode, wa, wb, o * COLS, FEAT, SHALF, gap)
            return bass.AP(state, off, [[SROW, P]] + half + [[1, COLS]])

        def state_all(mode, wa, wb, gap):
            off, half = halves(mode, wa, wb, 0, FEAT, SHALF, gap)
            return bass.AP(state, off, [[SROW, P]] + half + [[1, FEAT]])

        def xio_all(mode, wa, wb, gap):
            off, half = halves(mode, wa, wb, 0, 1, XHALF, gap)
            return bass.AP(xio, off, [[XROW, P]] + half + [[W, FEAT]])

        def split(mode, ap):
            return ap.rearrange("p (g c) -> p g c", g=2) if mode == "AB" else ap

        def norm_in(g, b, w0):
            ct, n = b // NG, b % NG
            off = g * XHALF + ct * COLS * W + n * H * W + w0
            return bass.AP(xio, off, [[XROW, P], [1, CHUNK], [W, H]])

        def norm_out(g, b, w0):
            ct, n = b // NG, b % NG
            off = g * SHALF + w0 * FEAT + ct * COLS + n * H
            return bass.AP(state, off, [[SROW, P], [FEAT, CHUNK], [1, H]])

        block = ctx.enter_context(nc.Block())

        def positions(j, phase, back=0):
            fa, ba = j + (1 - back), j * -1 + (STEPS - 1 + back)
            if phase == "lead":
                return "A", fa, None, 0
            if phase == "both forward":
                return "AB", fa, None, -SKEW
            if phase == "turn":
                return "AB", ba, None, fa - SKEW - ba
            if phase == "both backward":
                return "AB", ba, None, SKEW
            return "B", None, ba + SKEW, 0

        def loop(eng, first, last, body):
            n = (last - first) // 2
            if n > 1:
                with eng.Fori(first, first + 2 * n, 2) as j:
                    body(j, first % 2)
                    body(j + 1, (first + 1) % 2)
            elif n == 1:
                body(first, first % 2)
                body(first + 1, (first + 1) % 2)
            if (last - first) % 2:
                body(last - 1, (last - 1) % 2)

        @block.sync
        def _(sp):
            def load_x(n):
                sp.dma_start(xio[:, n // NG, :, (n % NG) * H:(n % NG + 1) * H, :],
                             x[n].rearrange("(t p) h w -> p t h w", p=P)).then_inc(x_loaded[n], 16)

            for n in range(NG):
                load_x(n)
            w_rows = conv_w.rearrange("(o p) i a b -> o p (i a b)", p=P)
            for o in range(KT):
                sp.dma_start(w_raw(o), w_rows[o]).then_inc(w_loaded[o], 16)
            sp.wait_ge(w_turned, 2)
            for n in range(NG, N):
                load_x(n)

            def store(n):
                sp.dma_start(out[n].rearrange("(t p) h w -> p t h w", p=P),
                             xio[:, n // NG, :, (n % NG) * H:(n % NG + 1) * H, :]).then_inc(stored, 16)

            sp.wait_ge(out_ready, 1)
            for n in range(NG):
                store(n)
            sp.wait_ge(out_ready, 2)
            for n in range(NG, N):
                store(n)
            sp.wait_ge(stored, 16 * N)

        @block.tensor
        def _(pe):
            pe.wait_ge(ident_done, 2)
            for o in range(KT):
                pe.wait_ge(w_loaded[o], 16)
                for k in range(KT):
                    t = nc.tensor.transpose(psum[:, o, k * P:(k + 1) * P], w_raw_block(o, k), ident[:, :])
                t.then_inc(w_turned, 1)
            pe.wait_ge(w_ready, KT)
            pe.wait_ge(norm_a, 1)

            def slot(phase):
                def body(j, par):
                    mode, wa, wb, gap = positions(j, phase, back=1)
                    c = cols(mode)
                    seen = set()
                    for k, o in UNITS:
                        if k not in seen:
                            seen.add(k)
                            if not (isinstance(j, int) and j == 0):
                                pe.wait_ge(state_ready, j * 4 + (k - 3))
                        mm = nc.tensor.matmul(psum[:, 4 * par + o, c], w_t[:, k, o * P:(o + 1) * P],
                                              state_tile(mode, wa, wb, gap, k), start=k == 0, stop=k == 3)
                        if k == 3:
                            mm.then_inc(tile_done, 1)
                return body

            slot("lead")(0, 0)
            loop(pe, 1, SKEW, slot("lead"))
            pe.wait_ge(norm_b, 1)
            loop(pe, SKEW, FWD + 1, slot("both forward"))
            for j in range(FWD + 1, FWD + SKEW + 1):
                slot("turn")(j, j % 2)
            loop(pe, FWD + SKEW + 1, STEPS, slot("both backward"))
            loop(pe, STEPS, LAST, slot("drain"))

        @block.scalar
        def _(act):
            with nc.allow_non_contiguous_dma(reason="512 biases, once"):
                act.dma_start(bias[:, :], conv_b.rearrange("(t p) -> p t", p=P)).then_inc(small_loaded, 16)
                act.dma_start(slope[:, :], prelu_a.partition_broadcast(P)).then_inc(small_loaded, 16)
            act.wait_ge(small_loaded, 32)
            nc.scalar.mul(neg_bias[:, :], bias[:, :], -1.0).then_inc(negated, 1)
            nc.scalar.mul(neg_slope[:, :], slope[:, :], -1.0).then_inc(negated, 1)
            act.wait_ge(negated, 2)
            for o in range(KT):
                act.wait_ge(w_turned, o + 1)
                nc.scalar.copy(w_t[:, :, o * P:(o + 1) * P],
                               psum[:, o, :].rearrange("p (k c) -> p k c", k=KT)).then_inc(w_ready, 1)

            def slot(mode):
                c = cols(mode)

                def body(j, par):
                    for o in range(KT):
                        act.wait_ge(tile_done, j * 4 + (o + 1))
                        z = psum[:, 4 * par + o, c]
                        nc.scalar.activation(above[:, par, o, c], z, ACT.Relu, bias=bias[:, o:o + 1],
                                             scale=1.0).then_inc(above_done, 1)
                        nc.scalar.activation(below[:, par, o, c], z, ACT.Relu, bias=neg_bias[:, o:o + 1],
                                             scale=-1.0).then_inc(below_done, 1)
                return body

            loop(act, 0, SKEW, slot("A"))
            loop(act, SKEW, STEPS, slot("AB"))
            loop(act, STEPS, LAST, slot("B"))

        @block.vector
        def _(dve):
            steps = [0]

            def chained(ins):
                ins.then_inc(stat_step, 1)
                steps[0] += 1
                dve.wait_ge(stat_step, steps[0])

            def block_stats(g, b, s):
                ct, n = b // NG, b % NG
                flat = bass.AP(xio, g * XHALF + ct * COLS * W + n * BLK + s * STAT, [[XROW, P], [1, STAT]])
                return nc.vector.bn_stats(bstat[:, b, s, :], flat)

            def group_stats(g):
                for b in range(NBLK):
                    last = nc.vector.bn_aggr(chan[:, 0, 2 * b:2 * b + 2],
                                             bstat[:, b, :, :].rearrange("p s v -> p (s v)"))
                chained(last)

                def spread(src, dst):
                    chained(nc.vector.transpose(chan_t[:, :, :].rearrange("p a b -> p (a b)"), src))
                    chained(nc.vector.reduce_sum(gsum[:, :], chan_t[:, :, :], axis=AXIS.X))
                    chained(nc.vector.tensor_scalar(
                        gsum_t[:, :, :], gsum[:, :].unsqueeze(2).to_broadcast([P, 2, 16]),
                        1.0 / GROUP, None, ALU.mult))
                    chained(nc.vector.transpose(dst, gsum_t[:, :, :].rearrange("p a b -> p (a b)")))

                def pairs(t):
                    return t.rearrange("p (b v) -> p b v", v=2)

                spread(chan[:, 0, :], gmean[:, :])
                chained(nc.vector.tensor_scalar(neg_mean[:, g, :], pairs(gmean[:, 0:2 * NBLK])[:, :, 0],
                                                -1.0, None, ALU.mult))
                chained(nc.vector.tensor_tensor(dev[:, 0:NBLK], pairs(chan[:, 0, 0:2 * NBLK])[:, :, 0],
                                                neg_mean[:, g, :], ALU.add))
                chained(nc.vector.tensor_tensor(dev[:, 0:NBLK], dev[:, 0:NBLK], dev[:, 0:NBLK], ALU.mult))
                spread(dev[:, :], gdev[:, :])
                nc.vector.scalar_tensor_tensor(var_eps[:, g, :], gdev[:, 0:NBLK], EPS,
                                               pairs(gmean[:, 0:2 * NBLK])[:, :, 1],
                                               ALU.add, ALU.add).then_inc(var_done, 1)

            def normalise(g, b, w0):
                return nc.vector.tensor_scalar(norm_out(g, b, w0), norm_in(g, b, w0),
                                               neg_mean[:, g, b:b + 1], rstd[:, g, b:b + 1],
                                               ALU.add, ALU.mult)

            chained(nc.vector.memset(chan[:, :, :], 0.0))
            chained(nc.vector.memset(dev[:, :], 0.0))
            nc.vector.memset(minus_half[:, :], -0.5).then_inc(zeroed, 1)
            for n in range(NG):
                dve.wait_ge(x_loaded[n], 16)
                for ct in range(KT):
                    for s in range(NSTAT):
                        last = block_stats(0, ct * NG + n, s)
            chained(last)
            group_stats(0)
            dve.wait_ge(rstd_done, 1)
            for w0 in range(0, W, CHUNK):
                for b in range(NBLK):
                    last = normalise(0, b, w0)
            last.then_inc(norm_a, 1)
            dve.wait_ge(negated, 2)

            def slot(phase):
                def body(j, par):
                    mode, wa, wb, gap = positions(j, phase)
                    c = cols(mode)

                    def part(o):
                        dve.wait_ge(above_done, j * 4 + (o + 1))
                        st = state_tile(mode, wa, wb, gap, o)
                        nc.vector.tensor_tensor(st, split(mode, above[:, par, o, c]), st,
                                                ALU.add).then_inc(part_done, 1)

                    def whole(o):
                        dve.wait_ge(below_done, j * 4 + (o + 1))
                        dve.wait_ge(part_done, j * 4 + (o + 1))
                        st = state_tile(mode, wa, wb, gap, o)
                        nc.vector.scalar_tensor_tensor(st, split(mode, below[:, par, o, c]), neg_slope[:, 0:1],
                                                       st, ALU.mult, ALU.add).then_inc(state_ready, 1)

                    for o in range(KT):
                        part(o)
                        whole(o)
                return body

            def add_input(j, mode, wa, wb, gap):
                dve.wait_ge(state_ready, j * 4 + 4)
                place = xio_all(mode, wa, wb, gap)
                return nc.vector.tensor_tensor(place, place, state_all(mode, wa, wb, gap), ALU.add)

            def slot_out(phase):
                def body(j, par):
                    slot(phase)(j, par)
                    add_input(j, *positions(j, phase))
                return body

            todo = [(b, s) for n in range(NG) for b in range(n, NBLK, NG) for s in range(NSTAT)]
            per = -(-len(todo) // SKEW)
            for j in range(SKEW):
                slot("lead")(j, j % 2)
                for b, s in todo[j * per:(j + 1) * per]:
                    dve.wait_ge(x_loaded[NG + b % NG], 16)
                    last = block_stats(1, b, s)
            chained(last)
            group_stats(1)
            dve.wait_ge(rstd_done, 2)
            for b in range(NBLK):
                last = normalise(1, b, 0)
            last.then_inc(norm_b, 1)
            dve.wait_ge(norm_b, 1)
            late = [(w0, b) for w0 in range(CHUNK, W, CHUNK) for b in range(NBLK)]
            per = -(-len(late) // (CHUNK - 1))
            for j in range(SKEW, SKEW + CHUNK - 1):
                slot("both forward")(j, j % 2)
                for w0, b in late[(j - SKEW) * per:(j - SKEW + 1) * per]:
                    last = normalise(1, b, w0)
            chained(last)
            loop(dve, SKEW + CHUNK - 1, FWD, slot("both forward"))
            add_input(FWD - 1, "A", W - 1, None, 0)
            for j in range(FWD, FWD + SKEW):
                slot("turn")(j, j % 2)
                add_input(j, "A", STEPS - 1 - j, None, 0)
            add_input(FWD + SKEW - 1, "B", None, W - 1, 0)
            loop(dve, FWD + SKEW, STEPS - 1, slot_out("both backward"))
            j = STEPS - 1
            slot("both backward")(j, j % 2)
            add_input(j, *positions(j, "both backward")).then_inc(out_ready, 1)
            loop(dve, STEPS, LAST - 1, slot_out("drain"))
            j = LAST - 1
            slot("drain")(j, j % 2)
            add_input(j, *positions(j, "drain")).then_inc(out_ready, 1)

        @block.gpsimd
        def _(pool):
            nc.gpsimd.memset(ident[:, :], 0.0).then_inc(ident_done, 1)
            pool.wait_ge(ident_done, 1)
            nc.gpsimd.affine_select(out=ident[:, :], in_=ident[:, :], compare_op=ALU.not_equal, fill=1.0,
                                    base=0, pattern=[[-1, P]], channel_multiplier=1).then_inc(ident_done, 1)

            def inverse_std(g):
                pool.wait_ge(zeroed, 1)
                pool.wait_ge(var_done, g + 1)
                nc.gpsimd.tensor_tensor(rstd[:, g, :], var_eps[:, g, :], minus_half[:, :],
                                        ALU.pow).then_inc(rstd_done, 1)

            inverse_std(0)
            inverse_std(1)


_INS = {"x": "x", "conv_w": "L0_conv_conv_w", "conv_b": "L0_conv_conv_b", "prelu_a": "L0_conv_prelu_a"}


def kernel(**inputs):
    import numpy as np
    import concourse.bacc as bacc
    from concourse.bass_utils import run_bass_kernel_spmd

    nc = bacc.Bacc("TRN2", target_bir_lowering=False, num_devices=1, dynamic_dma_scratch_size=1024)
    arrays, aps = {}, []
    for name, key in _INS.items():
        a = np.atleast_1d(np.ascontiguousarray(inputs[key]))
        arrays[f"in_{name}"] = a
        aps.append(nc.dram_tensor(f"in_{name}", a.shape, mybir.dt.from_np(a.dtype), kind="ExternalInput").ap())
    x = arrays["in_x"]
    out = nc.dram_tensor("out_y", x.shape, mybir.dt.from_np(x.dtype), kind="ExternalOutput").ap()
    scan_program(nc, *aps, out)
    r = run_bass_kernel_spmd(nc, [arrays], core_ids=[0])
    return r.results[0]["out_y"]
```

```python
from contextlib import ExitStack

import concourse.bass as bass
from concourse import mybir

ALU = mybir.AluOpType
ACT = mybir.ActivationFunctionType
AXIS = mybir.AxisListType
F32 = mybir.dt.float32
F32R = mybir.dt.float32r

P = 128
GROUP = 16
EPS = 1e-5
SKEW = 6

UNITS = [(0, 0), (0, 1), (0, 2), (0, 3), (1, 0), (1, 1), (1, 2), (2, 0), (3, 0),
         (2, 1), (3, 1), (2, 2), (3, 2), (1, 3), (2, 3), (3, 3)]
ORDER = [("part", 0), ("whole", 0), ("part", 1), ("part", 2), ("whole", 1), ("whole", 2), ("part", 3), ("whole", 3)]
UNROLL = 4
FIRST = 2
STATS_AFTER = [0, 2, 5, 9, 14, 19, 24]
WARM_UP = 24


def scan_program(nc, x, conv_w, conv_b, prelu_a, out):
    N, C, H, W = x.shape
    KT = C // P
    NG = N // 2
    COLS = NG * H
    TAPS = conv_w.shape[3]
    MID = TAPS // 2
    STEPS = 2 * (W - 1)
    FWD = W - 1
    LAST = STEPS + SKEW
    FEAT = KT * COLS
    BLK = H * W
    CHUNK = 12
    NBLK = KT * NG
    STAT = 512
    NSTAT = BLK // STAT
    assert KT == 4 and N == 4 and W % CHUNK == 0 and SKEW < CHUNK and SKEW % 2 == 0 and FWD % 2 == 1

    with ExitStack() as ctx:
        def sb(name, shape, dt=F32):
            return ctx.enter_context(nc.sbuf_tensor(name, shape, dt))

        def sem(name):
            return ctx.enter_context(nc.semaphore(name))

        xio = sb("xio", [P, 2, KT, COLS, W])
        state = sb("state", [P, 2, W, KT, COLS])
        w_t = sb("w_t", [P, KT, C])
        above = sb("above", [P, 2, KT, 2 * COLS])
        below = sb("below", [P, 2, KT, 2 * COLS])
        ident = sb("ident", [P, P])
        bias = sb("bias", [P, KT])
        neg_bias = sb("neg_bias", [P, KT])
        slope = sb("slope", [P, 1])
        neg_slope = sb("neg_slope", [P, 1])
        bstat = sb("bstat", [P, NBLK, NSTAT, 6])
        chan = sb("chan", [P, 2, 32])
        chan_t = sb("chan_t", [P, 2, 16])
        gsum = sb("gsum", [P, 2])
        gsum_t = sb("gsum_t", [P, 2, 16])
        gmean = sb("gmean", [P, 32])
        dev = sb("dev", [P, 32])
        gdev = sb("gdev", [P, 32])
        neg_mean = sb("neg_mean", [P, 2, NBLK])
        var_eps = sb("var_eps", [P, 2, NBLK])
        minus_half = sb("minus_half", [P, NBLK])
        rstd = sb("rstd", [P, 2, NBLK])
        psum = ctx.enter_context(nc.psum_tensor("psum", [P, 8, 512], F32))

        x_loaded = [[sem(f"x_loaded{n}_{t}") for t in range(KT)] for n in range(N)]
        w_loaded = [sem(f"w_loaded{o}") for o in range(KT)]
        small_loaded = sem("small_loaded")
        zeroed = sem("zeroed")
        ident_done = sem("ident_done")
        w_turned = sem("w_turned")
        w_ready = sem("w_ready")
        negated = sem("negated")
        stat_step = sem("stat_step")
        var_done = sem("var_done")
        rstd_done = sem("rstd_done")
        norm_a = sem("norm_a")
        norm_b = sem("norm_b")
        tile_done = sem("tile_done")
        above_done = sem("above_done")
        below_done = sem("below_done")
        part_done = sem("part_done")
        state_ready = sem("state_ready")
        out_ready = sem("out_ready")
        stored = sem("stored")

        SROW, XROW = 2 * W * FEAT, 2 * KT * COLS * W
        SHALF, XHALF = W * FEAT, KT * COLS * W

        def w_raw(o):
            t, room = (xio, XHALF) if o < 2 else (state, SHALF)
            base = room + (o % 2) * C * TAPS
            return bass.AP(t, base, [[SROW, P], [1, C * TAPS]])

        def w_raw_block(o, k):
            t, room = (xio, XHALF) if o < 2 else (state, SHALF)
            base = room + (o % 2) * C * TAPS + k * P * TAPS + MID
            return bass.AP(t, base, [[SROW, P], [TAPS, P]])

        def cols(mode):
            return {"A": slice(0, COLS), "B": slice(COLS, 2 * COLS), "AB": slice(0, 2 * COLS)}[mode]

        def halves(mode, wa, wb, base, step, whole, gap):
            if mode == "A":
                return wa * step + base, []
            if mode == "B":
                return wb * step + whole + base, []
            return wa * step + base, [[whole + gap * step, 2]]

        def moving(eng, mode, wa, wb, gap, k):
            if mode == "AB":
                return state_tile(eng, mode, wa, wb, gap, k)
            off, _ = halves(mode, wa, wb, k * COLS, FEAT, SHALF, gap)
            return bass.AP(state, reg(eng, off, 0, SROW - COLS), [[SROW, P], [0, 2], [1, COLS]])

        def reach(half):
            return half[0][0] if half else 0

        def state_tile(eng, mode, wa, wb, gap, o):
            off, half = halves(mode, wa, wb, o * COLS, FEAT, SHALF, gap)
            return bass.AP(state, reg(eng, off, 0, SROW - COLS - reach(half)), [[SROW, P]] + half + [[1, COLS]])

        def state_all(eng, mode, wa, wb, gap):
            off, half = halves(mode, wa, wb, 0, FEAT, SHALF, gap)
            return bass.AP(state, reg(eng, off, 0, SROW - FEAT - reach(half)), [[SROW, P]] + half + [[1, FEAT]])

        def xio_all(eng, mode, wa, wb, gap):
            off, half = halves(mode, wa, wb, 0, 1, XHALF, gap)
            return bass.AP(xio, reg(eng, off, 0, XROW - W * (FEAT - 1) - 1 - reach(half)), [[XROW, P]] + half + [[W, FEAT]])

        def split(mode, ap):
            return ap.rearrange("p (g c) -> p g c", g=2) if mode == "AB" else ap

        def norm_in(g, b, w0, w1):
            ct, n = b // NG, b % NG
            off = g * XHALF + ct * COLS * W + n * H * W + w0
            return bass.AP(xio, off, [[XROW, P], [1, w1 - w0], [W, H]])

        def norm_out(g, b, w0, w1):
            ct, n = b // NG, b % NG
            off = g * SHALF + w0 * FEAT + ct * COLS + n * H
            return bass.AP(state, off, [[SROW, P], [FEAT, w1 - w0], [1, H]])

        block = ctx.enter_context(nc.Block())

        def positions(j, phase, back=0):
            fa, ba = j + (1 - back), j * -1 + (STEPS - 1 + back)
            if phase == "lead":
                return "A", fa, None, 0
            if phase == "both forward":
                return "AB", fa, None, -SKEW
            if phase == "turn":
                return "AB", ba, None, fa - SKEW - ba
            if phase == "both backward":
                return "AB", ba, None, SKEW
            return "B", None, ba + SKEW, 0

        def loop(eng, first, last, body):
            n = (last - first) // UNROLL
            if n > 1:
                with eng.Fori(0, n) as turn:
                    for u in range(UNROLL):
                        body(turn * UNROLL + (first + u), (first + u) % 2)
                first += UNROLL * n
            for j in range(first, last):
                body(j, j % 2)

        def reg(eng, value, low, high):
            return value if isinstance(value, int) else eng.snap(value, min_val=low, max_val=high)

        def ready(eng, ap):
            eng.lower_ap(ap)
            return ap

        @block.sync
        def _(sp):
            def load_x(n):
                for t in range(KT):
                    sp.dma_start(xio[:, n // NG, t, (n % NG) * H:(n % NG + 1) * H, :],
                                 x[n, t * P:(t + 1) * P, :, :]).then_inc(x_loaded[n][t], 16)

            for n in range(NG):
                load_x(n)
            w_rows = conv_w.rearrange("(o p) i a b -> o p (i a b)", p=P)
            for o in range(KT):
                sp.dma_start(w_raw(o), w_rows[o]).then_inc(w_loaded[o], 16)
            sp.wait_ge(w_turned, 2)
            for n in range(NG, N):
                load_x(n)

            def store(n):
                sp.dma_start(out[n].rearrange("(t p) h w -> p t h w", p=P),
                             xio[:, n // NG, :, (n % NG) * H:(n % NG + 1) * H, :]).then_inc(stored, 16)

            sp.wait_ge(out_ready, 1)
            for n in range(NG):
                store(n)
            sp.wait_ge(out_ready, 2)
            for n in range(NG, N):
                store(n)
            sp.wait_ge(stored, 16 * N)

        @block.tensor
        def _(pe):
            pe.wait_ge(ident_done, 2)
            for o in range(KT):
                if o == KT - 1:
                    for _ in range(WARM_UP):
                        nc.tensor.matmul(psum[:, KT, 0:P], ident[:, :], ident[:, :], start=True, stop=True)
                pe.wait_ge(w_loaded[o], 16)
                for k in range(KT):
                    t = nc.tensor.transpose(psum[:, o, k * P:(k + 1) * P], w_raw_block(o, k), ident[:, :])
                t.then_inc(w_turned, 1)
            pe.wait_ge(w_ready, KT)
            pe.wait_ge(norm_a, 1)

            def slot(phase):
                def body(j, par):
                    mode, wa, wb, gap = positions(j, phase, back=1)
                    xs = [ready(pe, moving(pe, mode, wa, wb, gap, k)) for k in range(KT)]
                    before = [reg(pe, j * 4 + (k - 3), 1, 4 * LAST) for k in range(KT)]
                    seen = set()
                    for k, o in UNITS:
                        if k not in seen:
                            seen.add(k)
                            if not (isinstance(j, int) and j == 0):
                                pe.wait_ge(state_ready, before[k])
                        mm = nc.tensor.matmul(psum[:, 4 * par + o, 0:2 * COLS], w_t[:, k, o * P:(o + 1) * P],
                                              xs[k], start=k == 0, stop=k == 3)
                        if k == 3:
                            mm.then_inc(tile_done, 1)
                return body

            slot("lead")(0, 0)
            loop(pe, 1, SKEW, slot("lead"))
            pe.wait_ge(norm_b, 1)
            loop(pe, SKEW, FWD + 1, slot("both forward"))
            for j in range(FWD + 1, FWD + SKEW + 1):
                slot("turn")(j, j % 2)
            loop(pe, FWD + SKEW + 1, STEPS, slot("both backward"))
            loop(pe, STEPS, LAST, slot("drain"))

        @block.scalar
        def _(act):
            with nc.allow_non_contiguous_dma(reason="512 biases, once"):
                act.dma_start(bias[:, :], conv_b.rearrange("(t p) -> p t", p=P)).then_inc(small_loaded, 16)
                act.dma_start(slope[:, :], prelu_a.partition_broadcast(P)).then_inc(small_loaded, 16)
            act.wait_ge(small_loaded, 32)
            nc.scalar.mul(neg_bias[:, :], bias[:, :], -1.0).then_inc(negated, 1)
            nc.scalar.mul(neg_slope[:, :], slope[:, :], -1.0).then_inc(negated, 1)
            act.wait_ge(negated, 2)
            for o in range(KT):
                act.wait_ge(w_turned, o + 1)
                nc.scalar.copy(w_t[:, :, o * P:(o + 1) * P],
                               psum[:, o, :].rearrange("p (k c) -> p k c", k=KT)).then_inc(w_ready, 1)

            def slot(mode):
                c = cols(mode)

                def body(j, par):
                    nth = [reg(act, j * 4 + (o + 1), 1, 4 * LAST) for o in range(KT)]
                    for o in range(KT):
                        act.wait_ge(tile_done, nth[o])
                        z = psum[:, 4 * par + o, c]
                        nc.scalar.activation(above[:, par, o, c], z, ACT.Relu, bias=bias[:, o:o + 1],
                                             scale=1.0).then_inc(above_done, 1)
                        nc.scalar.activation(below[:, par, o, c], z, ACT.Relu, bias=neg_bias[:, o:o + 1],
                                             scale=-1.0).then_inc(below_done, 1)
                return body

            loop(act, 0, SKEW, slot("A"))
            loop(act, SKEW, STEPS, slot("AB"))
            loop(act, STEPS, LAST, slot("B"))

        @block.vector
        def _(dve):
            steps = [0]

            def chained(ins):
                ins.then_inc(stat_step, 1)
                steps[0] += 1
                dve.wait_ge(stat_step, steps[0])

            def block_stats(g, b, s):
                ct, n = b // NG, b % NG
                flat = bass.AP(xio, g * XHALF + ct * COLS * W + n * BLK + s * STAT, [[XROW, P], [1, STAT]])
                return nc.vector.bn_stats(bstat[:, b, s, :], flat)

            def group_stats(g):
                for b in range(NBLK):
                    last = nc.vector.bn_aggr(chan[:, 0, 2 * b:2 * b + 2],
                                             bstat[:, b, :, :].rearrange("p s v -> p (s v)"))
                chained(last)

                def spread(src, dst):
                    chained(nc.vector.transpose(chan_t[:, :, :].rearrange("p a b -> p (a b)"), src))
                    chained(nc.vector.reduce_sum(gsum[:, :], chan_t[:, :, :], axis=AXIS.X))
                    chained(nc.vector.tensor_scalar(
                        gsum_t[:, :, :], gsum[:, :].unsqueeze(2).to_broadcast([P, 2, 16]),
                        1.0 / GROUP, None, ALU.mult))
                    chained(nc.vector.transpose(dst, gsum_t[:, :, :].rearrange("p a b -> p (a b)")))

                def pairs(t):
                    return t.rearrange("p (b v) -> p b v", v=2)

                spread(chan[:, 0, :], gmean[:, :])
                chained(nc.vector.tensor_scalar(neg_mean[:, g, :], pairs(gmean[:, 0:2 * NBLK])[:, :, 0],
                                                -1.0, None, ALU.mult))
                chained(nc.vector.tensor_tensor(dev[:, 0:NBLK], pairs(chan[:, 0, 0:2 * NBLK])[:, :, 0],
                                                neg_mean[:, g, :], ALU.add))
                chained(nc.vector.tensor_tensor(dev[:, 0:NBLK], dev[:, 0:NBLK], dev[:, 0:NBLK], ALU.mult))
                spread(dev[:, :], gdev[:, :])
                nc.vector.scalar_tensor_tensor(var_eps[:, g, :], gdev[:, 0:NBLK], EPS,
                                               pairs(gmean[:, 0:2 * NBLK])[:, :, 1],
                                               ALU.add, ALU.add).then_inc(var_done, 1)

            def normalise(g, b, w0, w1):
                return nc.vector.tensor_scalar(norm_out(g, b, w0, w1), norm_in(g, b, w0, w1),
                                               neg_mean[:, g, b:b + 1], rstd[:, g, b:b + 1],
                                               ALU.add, ALU.mult)

            chained(nc.vector.memset(chan[:, :, :], 0.0))
            chained(nc.vector.memset(dev[:, :], 0.0))
            nc.vector.memset(minus_half[:, :], -0.5).then_inc(zeroed, 1)
            for n in range(NG):
                for ct in range(KT):
                    dve.wait_ge(x_loaded[n][ct], 16)
                    for s in range(NSTAT):
                        last = block_stats(0, ct * NG + n, s)
            chained(last)
            group_stats(0)
            dve.wait_ge(rstd_done, 1)
            for w0 in range(0, W, CHUNK):
                for b in range(NBLK):
                    last = normalise(0, b, w0, w0 + CHUNK)
                if w0 == 0:
                    last.then_inc(norm_a, 1)
            chained(last)
            dve.wait_ge(negated, 2)

            def slot(phase):
                def body(j, par):
                    mode, wa, wb, gap = positions(j, phase)
                    c = cols(mode)
                    sts = [ready(dve, state_tile(dve, mode, wa, wb, gap, o)) for o in range(KT)]
                    nth = [reg(dve, j * 4 + (o + 1), 1, 4 * LAST) for o in range(KT)]

                    def part(o):
                        dve.wait_ge(above_done, nth[o])
                        nc.vector.tensor_tensor(sts[o], split(mode, above[:, par, o, c]), sts[o],
                                                ALU.add).then_inc(part_done, 1)

                    def whole(o):
                        dve.wait_ge(below_done, nth[o])
                        dve.wait_ge(part_done, nth[o])
                        nc.vector.scalar_tensor_tensor(sts[o], split(mode, below[:, par, o, c]),
                                                       neg_slope[:, 0:1], sts[o], ALU.mult, ALU.add).then_inc(state_ready, 1)

                    for step, o in ORDER:
                        (part if step == "part" else whole)(o)
                return body

            def add_input(j, mode, wa, wb, gap):
                place = ready(dve, xio_all(dve, mode, wa, wb, gap))
                result = ready(dve, state_all(dve, mode, wa, wb, gap))
                dve.wait_ge(state_ready, j * 4 + 4)
                return nc.vector.tensor_tensor(place, place, result, ALU.add)

            def slot_out(phase):
                def body(j, par):
                    slot(phase)(j, par)
                    add_input(j, *positions(j, phase))
                return body

            todo = [(n, ct, s) for n in range(NG) for ct in range(KT) for s in range(NSTAT)]
            for j in range(SKEW):
                slot("lead")(j, j % 2)
                for n, ct, s in todo[STATS_AFTER[j]:STATS_AFTER[j + 1]]:
                    if s == 0:
                        dve.wait_ge(x_loaded[NG + n][ct], 16)
                    last = block_stats(1, ct * NG + n, s)
            chained(last)
            group_stats(1)
            dve.wait_ge(rstd_done, 2)
            for b in range(NBLK):
                last = normalise(1, b, 0, FIRST)
            last.then_inc(norm_b, 1)
            for b in range(NBLK):
                last = normalise(1, b, FIRST, CHUNK)
            chained(last)
            late = [(w0, b) for w0 in range(CHUNK, W, CHUNK) for b in range(NBLK)]
            per = -(-len(late) // (CHUNK - 1))
            for j in range(SKEW, SKEW + CHUNK - 1):
                slot("both forward")(j, j % 2)
                for w0, b in late[(j - SKEW) * per:(j - SKEW + 1) * per]:
                    last = normalise(1, b, w0, w0 + CHUNK)
            chained(last)
            loop(dve, SKEW + CHUNK - 1, FWD, slot("both forward"))
            add_input(FWD - 1, "A", W - 1, None, 0)
            for j in range(FWD, FWD + SKEW):
                slot("turn")(j, j % 2)
                add_input(j, "A", STEPS - 1 - j, None, 0)
            add_input(FWD + SKEW - 1, "B", None, W - 1, 0)
            loop(dve, FWD + SKEW, STEPS - 1, slot_out("both backward"))
            j = STEPS - 1
            slot("both backward")(j, j % 2)
            add_input(j, *positions(j, "both backward")).then_inc(out_ready, 1)
            loop(dve, STEPS, LAST - 1, slot_out("drain"))
            j = LAST - 1
            slot("drain")(j, j % 2)
            add_input(j, *positions(j, "drain")).then_inc(out_ready, 1)

        @block.gpsimd
        def _(pool):
            nc.gpsimd.memset(ident[:, :], 0.0).then_inc(ident_done, 1)
            pool.wait_ge(ident_done, 1)
            nc.gpsimd.affine_select(out=ident[:, :], in_=ident[:, :], compare_op=ALU.not_equal, fill=1.0,
                                    base=0, pattern=[[-1, P]], channel_multiplier=1).then_inc(ident_done, 1)

            def inverse_std(g):
                pool.wait_ge(zeroed, 1)
                pool.wait_ge(var_done, g + 1)
                nc.gpsimd.tensor_tensor(rstd[:, g, :], var_eps[:, g, :], minus_half[:, :],
                                        ALU.pow).then_inc(rstd_done, 1)

            inverse_std(0)
            inverse_std(1)


_INS = {"x": "x", "conv_w": "L0_conv_conv_w", "conv_b": "L0_conv_conv_b", "prelu_a": "L0_conv_prelu_a"}


def kernel(**inputs):
    import numpy as np
    import concourse.bacc as bacc
    from concourse.bass_utils import run_bass_kernel_spmd

    nc = bacc.Bacc("TRN2", target_bir_lowering=False, num_devices=1, dynamic_dma_scratch_size=1024)
    arrays, aps = {}, []
    for name, key in _INS.items():
        a = np.atleast_1d(np.ascontiguousarray(inputs[key]))
        arrays[f"in_{name}"] = a
        aps.append(nc.dram_tensor(f"in_{name}", a.shape, mybir.dt.from_np(a.dtype), kind="ExternalInput").ap())
    x = arrays["in_x"]
    out = nc.dram_tensor("out_y", x.shape, mybir.dt.from_np(x.dtype), kind="ExternalOutput").ap()
    scan_program(nc, *aps, out)
    r = run_bass_kernel_spmd(nc, [arrays], core_ids=[0])
    return r.results[0]["out_y"]
```

```python
from contextlib import ExitStack

import concourse.bass as bass
from concourse import mybir

ALU = mybir.AluOpType
ACT = mybir.ActivationFunctionType
AXIS = mybir.AxisListType
F32 = mybir.dt.float32

P = 128
GROUP = 16
EPS = 1e-5
SKEW = 5

UNITS = [(0, 0), (0, 1), (0, 2), (0, 3), (1, 0), (1, 1), (1, 2), (2, 0), (3, 0),
         (2, 1), (3, 1), (2, 2), (3, 2), (1, 3), (2, 3), (3, 3)]
ORDER = [("part", 0), ("whole", 0), ("part", 1), ("part", 2), ("whole", 1), ("whole", 2), ("part", 3), ("whole", 3)]
UNROLL = 2
NEXT = 4
BY_ACT = [(0, 1), (1, 1)]
STATS = [3, 4, 4, 4, 3]
WARM_UP = 24
KEEP_UP = 16


def scan_program(nc, x, conv_w, conv_b, prelu_a, out):
    N, C, H, W = x.shape
    KT = C // P
    NG = N // 2
    COLS = NG * H
    TAPS = conv_w.shape[3]
    MID = TAPS // 2
    STEPS = 2 * (W - 1)
    FWD = W - 1
    LAST = STEPS + SKEW
    FEAT = KT * COLS
    BLK = H * W
    CHUNK = 12
    NBLK = KT * NG
    STAT = 512
    NSTAT = BLK // STAT
    assert KT == 4 and N == 4 and W % CHUNK == 0 and SKEW < CHUNK and FWD % 2 == 1

    with ExitStack() as ctx:
        def sb(name, shape, dt=F32):
            return ctx.enter_context(nc.sbuf_tensor(name, shape, dt))

        def sem(name):
            return ctx.enter_context(nc.semaphore(name))

        xio = sb("xio", [P, 2, KT, COLS, W])
        state = sb("state", [P, 2, W, KT, COLS])
        w_t = sb("w_t", [P, KT, C])
        above = sb("above", [P, 2, KT, 2 * COLS])
        below = sb("below", [P, 2, KT, 2 * COLS])
        ident = sb("ident", [P, P])
        bias = sb("bias", [P, KT])
        neg_bias = sb("neg_bias", [P, KT])
        slope = sb("slope", [P, 1])
        neg_slope = sb("neg_slope", [P, 1])
        bstat = sb("bstat", [P, NBLK, NSTAT, 6])
        chan = sb("chan", [P, 2, 32])
        chan_t = sb("chan_t", [P, 2, 2, 16])
        piece_sum = sb("piece_sum", [P, 2, NSTAT])
        scaled = sb("scaled", [P, NSTAT])
        gsum = sb("gsum", [P, 2, 2])
        dev = sb("dev", [P, 2, 16])
        dev_sum = sb("dev_sum", [P, 2])
        var_sum = sb("var_sum", [P, 2])
        inv_root = sb("inv_root", [P, 2])
        minus_half = sb("minus_half", [P, 2])
        group_t = sb("group_t", [P, 2, 2, 16])
        gstat = sb("gstat", [P, 2, 2, 32])
        psum = ctx.enter_context(nc.psum_tensor("psum", [P, 8, 512], F32))

        x_loaded = [[sem(f"x_loaded{n}_{t}") for t in range(KT)] for n in range(N)]
        w_loaded = [sem(f"w_loaded{o}") for o in range(KT)]
        small_loaded = sem("small_loaded")
        zeroed = sem("zeroed")
        ident_done = sem("ident_done")
        w_turned = sem("w_turned")
        w_ready = sem("w_ready")
        negated = sem("negated")
        stat_step = sem("stat_step")
        act_step = sem("act_step")
        act_stats = sem("act_stats")
        most_stats = sem("most_stats")
        var_done = sem("var_done")
        rstd_done = sem("rstd_done")
        norm_a = sem("norm_a")
        norm_b = sem("norm_b")
        tile_done = sem("tile_done")
        above_done = sem("above_done")
        below_done = sem("below_done")
        part_done = sem("part_done")
        state_ready = sem("state_ready")
        out_ready = sem("out_ready")
        stored = sem("stored")

        SROW, XROW = 2 * W * FEAT, 2 * KT * COLS * W
        SHALF, XHALF = W * FEAT, KT * COLS * W

        def w_raw(o):
            t, room = (xio, XHALF) if o < 2 else (state, SHALF)
            base = room + (o % 2) * C * TAPS
            return bass.AP(t, base, [[SROW, P], [1, C * TAPS]])

        def w_raw_block(o, k):
            t, room = (xio, XHALF) if o < 2 else (state, SHALF)
            base = room + (o % 2) * C * TAPS + k * P * TAPS + MID
            return bass.AP(t, base, [[SROW, P], [TAPS, P]])

        def x_piece(g, n, ct, s):
            return bass.AP(xio, g * XHALF + ct * COLS * W + n * BLK + s * STAT, [[XROW, P], [1, STAT]])

        def cols(mode):
            return {"A": slice(0, COLS), "B": slice(COLS, 2 * COLS), "AB": slice(0, 2 * COLS)}[mode]

        def halves(mode, wa, wb, base, step, whole, gap):
            if mode == "A":
                return wa * step + base, []
            if mode == "B":
                return wb * step + whole + base, []
            return wa * step + base, [[whole + gap * step, 2]]

        def moving(eng, mode, wa, wb, gap, k):
            if mode == "AB":
                return state_tile(eng, mode, wa, wb, gap, k)
            off, _ = halves(mode, wa, wb, k * COLS, FEAT, SHALF, gap)
            return bass.AP(state, reg(eng, off, 0, SROW - COLS), [[SROW, P], [0, 2], [1, COLS]])

        def reach(half):
            return half[0][0] if half else 0

        def state_tile(eng, mode, wa, wb, gap, o):
            off, half = halves(mode, wa, wb, o * COLS, FEAT, SHALF, gap)
            return bass.AP(state, reg(eng, off, 0, SROW - COLS - reach(half)), [[SROW, P]] + half + [[1, COLS]])

        def state_all(eng, mode, wa, wb, gap):
            off, half = halves(mode, wa, wb, 0, FEAT, SHALF, gap)
            return bass.AP(state, reg(eng, off, 0, SROW - FEAT - reach(half)), [[SROW, P]] + half + [[1, FEAT]])

        def xio_all(eng, mode, wa, wb, gap):
            off, half = halves(mode, wa, wb, 0, 1, XHALF, gap)
            return bass.AP(xio, reg(eng, off, 0, XROW - W * (FEAT - 1) - 1 - reach(half)), [[XROW, P]] + half + [[W, FEAT]])

        def split(mode, ap):
            return ap.rearrange("p (g c) -> p g c", g=2) if mode == "AB" else ap

        def norm_in(g, b, w0, w1):
            ct, n = b // NG, b % NG
            off = g * XHALF + ct * COLS * W + n * H * W + w0
            return bass.AP(xio, off, [[XROW, P], [1, w1 - w0], [W, H]])

        def norm_out(g, b, w0, w1):
            ct, n = b // NG, b % NG
            off = g * SHALF + w0 * FEAT + ct * COLS + n * H
            return bass.AP(state, off, [[SROW, P], [FEAT, w1 - w0], [1, H]])

        block = ctx.enter_context(nc.Block())

        def positions(j, phase, back=0):
            fa, ba = j + (1 - back), j * -1 + (STEPS - 1 + back)
            if phase == "lead":
                return "A", fa, None, 0
            if phase == "both forward":
                return "AB", fa, None, -SKEW
            if phase == "turn":
                return "AB", ba, None, fa - SKEW - ba
            if phase == "both backward":
                return "AB", ba, None, SKEW
            return "B", None, ba + SKEW, 0

        def loop(eng, first, last, body):
            n = (last - first) // UNROLL
            if n > 1:
                with eng.Fori(0, n) as turn:
                    for u in range(UNROLL):
                        body(turn * UNROLL + (first + u), (first + u) % 2)
                first += UNROLL * n
            for j in range(first, last):
                body(j, j % 2)

        def reg(eng, value, low, high):
            return value if isinstance(value, int) else eng.snap(value, min_val=low, max_val=high)

        def ready(eng, ap):
            eng.lower_ap(ap)
            return ap

        @block.sync
        def _(sp):
            def load_x(n):
                for t in range(KT):
                    sp.dma_start(xio[:, n // NG, t, (n % NG) * H:(n % NG + 1) * H, :],
                                 x[n, t * P:(t + 1) * P, :, :]).then_inc(x_loaded[n][t], 16)

            for n in range(NG):
                load_x(n)
            w_rows = conv_w.rearrange("(o p) i a b -> o p (i a b)", p=P)
            for o in range(KT):
                sp.dma_start(w_raw(o), w_rows[o]).then_inc(w_loaded[o], 16)
            sp.wait_ge(w_turned, 2)
            for n in range(NG, N):
                load_x(n)

            def store(n):
                sp.dma_start(out[n].rearrange("(t p) h w -> p t h w", p=P),
                             xio[:, n // NG, :, (n % NG) * H:(n % NG + 1) * H, :]).then_inc(stored, 16)

            sp.wait_ge(out_ready, 1)
            for n in range(NG):
                store(n)
            sp.wait_ge(out_ready, 2)
            for n in range(NG, N):
                store(n)
            sp.wait_ge(stored, 16 * N)

        @block.tensor
        def _(pe):
            pe.wait_ge(ident_done, 2)
            for o in range(KT):
                if o == KT - 1:
                    for _ in range(WARM_UP):
                        nc.tensor.matmul(psum[:, KT, 0:P], ident[:, :], ident[:, :], start=True, stop=True)
                pe.wait_ge(w_loaded[o], 16)
                for k in range(KT):
                    t = nc.tensor.transpose(psum[:, o, k * P:(k + 1) * P], w_raw_block(o, k), ident[:, :])
                t.then_inc(w_turned, 1)
            pe.wait_ge(w_ready, KT)
            pe.wait_ge(norm_a, 1)

            def slot(phase):
                def body(j, par):
                    mode, wa, wb, gap = positions(j, phase, back=1)
                    xs = [ready(pe, moving(pe, mode, wa, wb, gap, k)) for k in range(KT)]
                    before = [reg(pe, j * 4 + (k - 3), 1, 4 * LAST) for k in range(KT)]
                    seen = set()
                    for k, o in UNITS:
                        if k not in seen:
                            seen.add(k)
                            if not (isinstance(j, int) and j == 0):
                                pe.wait_ge(state_ready, before[k])
                        mm = nc.tensor.matmul(psum[:, 4 * par + o, 0:2 * COLS], w_t[:, k, o * P:(o + 1) * P],
                                              xs[k], start=k == 0, stop=k == 3)
                        if k == 3:
                            mm.then_inc(tile_done, 1)
                return body

            slot("lead")(0, 0)
            loop(pe, 1, SKEW, slot("lead"))
            for _ in range(KEEP_UP):
                nc.tensor.matmul(psum[:, 4 * (SKEW % 2), 0:P], ident[:, :], ident[:, :], start=True, stop=True)
            pe.wait_ge(norm_b, 1)
            slot("both forward")(SKEW, SKEW % 2)
            loop(pe, SKEW + 1, FWD + 1, slot("both forward"))
            for j in range(FWD + 1, FWD + SKEW + 1):
                slot("turn")(j, j % 2)
            loop(pe, FWD + SKEW + 1, STEPS, slot("both backward"))
            loop(pe, STEPS, LAST, slot("drain"))

        @block.scalar
        def _(act):
            with nc.allow_non_contiguous_dma(reason="512 biases, once"):
                act.dma_start(bias[:, :], conv_b.rearrange("(t p) -> p t", p=P)).then_inc(small_loaded, 16)
                act.dma_start(slope[:, :], prelu_a.partition_broadcast(P)).then_inc(small_loaded, 16)
            act.wait_ge(small_loaded, 32)
            nc.scalar.mul(neg_bias[:, :], bias[:, :], -1.0).then_inc(negated, 1)
            nc.scalar.mul(neg_slope[:, :], slope[:, :], -1.0).then_inc(negated, 1)
            act.wait_ge(negated, 2)
            for o in range(KT):
                act.wait_ge(w_turned, o + 1)
                nc.scalar.copy(w_t[:, :, o * P:(o + 1) * P],
                               psum[:, o, :].rearrange("p (k c) -> p k c", k=KT)).then_inc(w_ready, 1)

            def slot(mode):
                c = cols(mode)

                def body(j, par):
                    nth = [reg(act, j * 4 + (o + 1), 1, 4 * LAST) for o in range(KT)]
                    for o in range(KT):
                        act.wait_ge(tile_done, nth[o])
                        z = psum[:, 4 * par + o, c]
                        nc.scalar.activation(above[:, par, o, c], z, ACT.Relu, bias=bias[:, o:o + 1],
                                             scale=1.0).then_inc(above_done, 1)
                        nc.scalar.activation(below[:, par, o, c], z, ACT.Relu, bias=neg_bias[:, o:o + 1],
                                             scale=-1.0).then_inc(below_done, 1)
                return body

            steps = [0]

            def chained(ins):
                ins.then_inc(act_step, 1)
                steps[0] += 1
                act.wait_ge(act_step, steps[0])

            def pieces(n, ct, kind):
                b = ct * NG + n
                junk = bass.AP(state, SHALF + 2 * C * TAPS, [[SROW, P], [1, STAT]])
                for s in range(NSTAT):
                    if kind == 0:
                        last = nc.scalar.activation(junk, x_piece(1, n, ct, s), ACT.Identity,
                                                    accum_out=piece_sum[:, 0, s:s + 1])
                    else:
                        last = nc.scalar.activation(junk, x_piece(1, n, ct, s), ACT.Square, scale=-1.0,
                                                    bias=chan[:, 0, b:b + 1], accum_out=piece_sum[:, 1, s:s + 1])
                    chained(last)
                return nc.scalar.activation(scaled[:, :], piece_sum[:, kind, :], ACT.Identity,
                                            scale=1.0 / BLK, accum_out=chan[:, kind, b:b + 1])

            act.wait_ge(zeroed, 1)
            for j in range(SKEW):
                slot("A")(j, j % 2)
                if j // 2 < len(BY_ACT):
                    n, ct = BY_ACT[j // 2]
                    if j % 2 == 0:
                        act.wait_ge(x_loaded[NG + n][ct], 16)
                    last = pieces(n, ct, j % 2)
                    if j % 2 == 0:
                        chained(last)
                    else:
                        last.then_inc(act_stats, 1)
            loop(act, SKEW, STEPS, slot("AB"))
            loop(act, STEPS, LAST, slot("B"))

        @block.vector
        def _(dve):
            steps = [0]

            def chained(ins):
                ins.then_inc(stat_step, 1)
                steps[0] += 1
                dve.wait_ge(stat_step, steps[0])

            def block_stats(g, b, s):
                return nc.vector.bn_stats(bstat[:, b, s, :], x_piece(g, b % NG, b // NG, s))

            def aggregate(b):
                return nc.vector.bn_aggr(chan[:, :, b], bstat[:, b, :, :].rearrange("p s v -> p (s v)"))

            def group_stats(g):
                chained(nc.vector.transpose(chan_t[:, :, :, :].rearrange("p v a c -> p (v a c)"),
                                            chan[:, :, :].rearrange("p v b -> p (v b)")))
                chained(nc.vector.reduce_sum(gsum[:, :, :], chan_t[:, :, :, :], axis=AXIS.X))
                chained(nc.vector.scalar_tensor_tensor(
                    dev[:, :, :], gsum[:, 0, :].unsqueeze(2).to_broadcast([P, 2, GROUP]), 1.0 / GROUP,
                    chan_t[:, 0, :, :], ALU.mult, ALU.subtract))
                chained(nc.vector.tensor_tensor(dev[:, :, :], dev[:, :, :], dev[:, :, :], ALU.mult))
                chained(nc.vector.reduce_sum(dev_sum[:, :], dev[:, :, :], axis=AXIS.X))
                nc.vector.scalar_tensor_tensor(var_sum[:, :], dev_sum[:, :], GROUP * EPS, gsum[:, 1, :],
                                               ALU.add, ALU.add).then_inc(var_done, 1)
                nc.vector.tensor_scalar(group_t[:, 0, :, :], gsum[:, 0, :].unsqueeze(2).to_broadcast([P, 2, GROUP]),
                                        1.0 / GROUP, None, ALU.mult)
                dve.wait_ge(rstd_done, g + 1)
                chained(nc.vector.tensor_scalar(
                    group_t[:, 1, :, :], inv_root[:, :].unsqueeze(2).to_broadcast([P, 2, GROUP]),
                    float(GROUP) ** 0.5, None, ALU.mult))
                chained(nc.vector.transpose(gstat[:, g, :, :].rearrange("p v b -> p (v b)"),
                                            group_t[:, :, :, :].rearrange("p v a c -> p (v a c)")))

            def normalise(g, b, w0, w1):
                return nc.vector.tensor_scalar(norm_out(g, b, w0, w1), norm_in(g, b, w0, w1),
                                               gstat[:, g, 0, b:b + 1], gstat[:, g, 1, b:b + 1],
                                               ALU.subtract, ALU.mult)

            def normalise_first(g):
                x_0 = bass.AP(xio, g * XHALF, [[XROW, P], [H * W, NBLK], [W, H]])
                out_0 = bass.AP(state, g * SHALF, [[SROW, P], [H, NBLK], [1, H]])
                mean, rstd = (gstat[:, g, v, 0:NBLK].unsqueeze(2).to_broadcast([P, NBLK, H]) for v in range(2))
                chained(nc.vector.tensor_tensor(out_0, x_0, mean, ALU.subtract))
                return nc.vector.tensor_tensor(out_0, out_0, rstd, ALU.mult)

            chained(nc.vector.memset(chan[:, :, :], 0.0))
            nc.vector.memset(minus_half[:, :], -0.5).then_inc(zeroed, 1)
            for n in range(NG):
                for ct in range(KT):
                    dve.wait_ge(x_loaded[n][ct], 16)
                    for s in range(NSTAT):
                        last = block_stats(0, ct * NG + n, s)
            chained(last)
            for b in range(NBLK):
                last = aggregate(b)
            chained(last)
            group_stats(0)
            for w0 in range(0, W, CHUNK):
                for b in range(NBLK):
                    last = normalise(0, b, w0, w0 + CHUNK)
                if w0 == 0:
                    last.then_inc(norm_a, 1)
            chained(last)

            def stats_b(blocks):
                for n, ct, s in blocks:
                    if s == 0:
                        dve.wait_ge(x_loaded[NG + n][ct], 16)
                    last = block_stats(1, ct * NG + n, s)
                return last

            dve.wait_ge(negated, 2)

            def slot(phase):
                def body(j, par):
                    mode, wa, wb, gap = positions(j, phase)
                    c = cols(mode)
                    sts = [ready(dve, state_tile(dve, mode, wa, wb, gap, o)) for o in range(KT)]
                    nth = [reg(dve, j * 4 + (o + 1), 1, 4 * LAST) for o in range(KT)]

                    def part(o):
                        dve.wait_ge(above_done, nth[o])
                        nc.vector.tensor_tensor(sts[o], split(mode, above[:, par, o, c]), sts[o],
                                                ALU.add).then_inc(part_done, 1)

                    def whole(o):
                        dve.wait_ge(part_done, nth[o])
                        dve.wait_ge(below_done, nth[o])
                        nc.vector.scalar_tensor_tensor(sts[o], split(mode, below[:, par, o, c]),
                                                       neg_slope[:, 0:1], sts[o], ALU.mult, ALU.add).then_inc(state_ready, 1)

                    for step, o in ORDER:
                        (part if step == "part" else whole)(o)
                return body

            def add_input(j, mode, wa, wb, gap):
                place = ready(dve, xio_all(dve, mode, wa, wb, gap))
                result = ready(dve, state_all(dve, mode, wa, wb, gap))
                dve.wait_ge(state_ready, j * 4 + 4)
                return nc.vector.tensor_tensor(place, place, result, ALU.add)

            def slot_out(phase):
                def body(j, par):
                    slot(phase)(j, par)
                    add_input(j, *positions(j, phase))
                return body

            def lead(j):
                for o in range(KT):
                    dve.wait_ge(part_done, j * 4 + (o + 1))
                    dve.wait_ge(below_done, j * 4 + (o + 1))
                    st = state_tile(dve, "A", j + 1, None, 0, o)
                    nc.vector.scalar_tensor_tensor(st, below[:, j % 2, o, 0:COLS], neg_slope[:, 0:1], st,
                                                   ALU.mult, ALU.add).then_inc(state_ready, 1)

            todo = [(n, ct) for n in range(NG) for ct in range(KT) if (n, ct) not in BY_ACT]
            pieces = [(n, ct, s) for n, ct in todo for s in range(NSTAT)]
            stats_b(pieces[:STATS[0]])
            for j in range(SKEW - 2):
                lead(j)
                done = sum(STATS[:j + 1])
                last = stats_b(pieces[done:done + STATS[j + 1]])
            last.then_inc(most_stats, 1)
            lead(SKEW - 2)
            done = sum(STATS[:SKEW - 1])
            dve.wait_ge(most_stats, 1)
            for n, ct in todo[:done // NSTAT]:
                aggregate(ct * NG + n)
            chained(stats_b(pieces[done:]))
            for n, ct in todo[done // NSTAT:]:
                last = aggregate(ct * NG + n)
            dve.wait_ge(act_stats, len(BY_ACT))
            chained(last)
            group_stats(1)
            normalise_first(1).then_inc(norm_b, 1)
            lead(SKEW - 1)
            for b in range(NBLK):
                last = normalise(1, b, 1, NEXT)
            chained(last)
            late = [(w0, w1, b) for w0, w1 in [(NEXT, CHUNK)] + [(w, w + CHUNK) for w in range(CHUNK, W, CHUNK)]
                    for b in range(NBLK)]
            per = -(-len(late) // (CHUNK - 1))
            for j in range(SKEW, SKEW + CHUNK - 1):
                slot("both forward")(j, j % 2)
                for w0, w1, b in late[(j - SKEW) * per:(j - SKEW + 1) * per]:
                    last = normalise(1, b, w0, w1)
                if j - SKEW + 1 == NEXT - 1:
                    chained(last)
            chained(last)
            loop(dve, SKEW + CHUNK - 1, FWD, slot("both forward"))
            add_input(FWD - 1, "A", W - 1, None, 0)
            for j in range(FWD, FWD + SKEW):
                slot("turn")(j, j % 2)
                add_input(j, "A", STEPS - 1 - j, None, 0)
            add_input(FWD + SKEW - 1, "B", None, W - 1, 0)
            loop(dve, FWD + SKEW, STEPS - 1, slot_out("both backward"))
            j = STEPS - 1
            slot("both backward")(j, j % 2)
            add_input(j, *positions(j, "both backward")).then_inc(out_ready, 1)
            loop(dve, STEPS, LAST - 1, slot_out("drain"))
            j = LAST - 1
            slot("drain")(j, j % 2)
            add_input(j, *positions(j, "drain")).then_inc(out_ready, 1)

        @block.gpsimd
        def _(pool):
            nc.gpsimd.memset(ident[:, :], 0.0).then_inc(ident_done, 1)
            pool.wait_ge(ident_done, 1)
            nc.gpsimd.affine_select(out=ident[:, :], in_=ident[:, :], compare_op=ALU.not_equal, fill=1.0,
                                    base=0, pattern=[[-1, P]], channel_multiplier=1).then_inc(ident_done, 1)

            def inverse_root(g):
                pool.wait_ge(zeroed, 1)
                pool.wait_ge(var_done, g + 1)
                nc.gpsimd.tensor_tensor(inv_root[:, :], var_sum[:, :], minus_half[:, :],
                                        ALU.pow).then_inc(rstd_done, 1)

            def lead(j):
                for o in range(KT):
                    pool.wait_ge(above_done, j * 4 + (o + 1))
                    st = state_tile(pool, "A", j + 1, None, 0, o)
                    nc.gpsimd.tensor_tensor(st, above[:, j % 2, o, 0:COLS], st, ALU.add).then_inc(part_done, 1)

            inverse_root(0)
            pool.wait_ge(norm_a, 1)
            for j in range(SKEW - 1):
                lead(j)
            inverse_root(1)
            lead(SKEW - 1)


_INS = {"x": "x", "conv_w": "L0_conv_conv_w", "conv_b": "L0_conv_conv_b", "prelu_a": "L0_conv_prelu_a"}


def kernel(**inputs):
    import numpy as np
    import concourse.bacc as bacc
    from concourse.bass_utils import run_bass_kernel_spmd

    nc = bacc.Bacc("TRN2", target_bir_lowering=False, num_devices=1, dynamic_dma_scratch_size=1024)
    arrays, aps = {}, []
    for name, key in _INS.items():
        a = np.atleast_1d(np.ascontiguousarray(inputs[key]))
        arrays[f"in_{name}"] = a
        aps.append(nc.dram_tensor(f"in_{name}", a.shape, mybir.dt.from_np(a.dtype), kind="ExternalInput").ap())
    x = arrays["in_x"]
    out = nc.dram_tensor("out_y", x.shape, mybir.dt.from_np(x.dtype), kind="ExternalOutput").ap()
    scan_program(nc, *aps, out)
    r = run_bass_kernel_spmd(nc, [arrays], core_ids=[0])
    return r.results[0]["out_y"]
```
